# Optimizing a Trainium2 kernel written in Bass

```python
import numpy as np
import jax
import jax.numpy as jnp

def _softmax(x, axis=-1):
    return jax.nn.softmax(x, axis=axis)
def _gelu(x):
    return jax.nn.gelu(x, approximate=True)
def _silu(x):
    return jax.nn.silu(x)
def _sigmoid(x):
    return jax.nn.sigmoid(x)
def _layernorm(x, axis=-1, eps=1e-5):
    m = jnp.mean(x, axis=axis, keepdims=True)
    v = jnp.var(x, axis=axis, keepdims=True)
    return (x - m) / jnp.sqrt(v + eps)
def _scatter_add(tgt, idx, src, axis=0):
    return tgt.at[idx].add(src)
def _segment_sum(src, seg, n):
    return jax.ops.segment_sum(src, seg, n)

kernel_name = 'mk_adj_preln_d1_adj_1024_4cb900'

def setup_inputs(seed: int = 0):
    np.random.seed(seed)
    _w = jnp.asarray
    def _rec_inputs():
        import jax
        import jax.numpy as jnp
        _gk = jax.random.key(seed)
        x = -0.0002928 + 1 * jax.random.normal(jax.random.fold_in(_gk, 1), (32, 512, 1024), jnp.float32)
        _w = (1.0 + jnp.arange(512, dtype=jnp.float32)) ** -0.5
        _w = _w / _w.mean()
        _pij = jnp.clip(0.015625 * _w[:, None] * _w[None, :], 0.0, 1.0)
        _a = jax.random.uniform(jax.random.fold_in(_gk, 2), (32, 512, 512)) < _pij
        adj = _a.astype(jnp.int32)
        return x, adj
    x, adj = _rec_inputs()
    def _L0_gnn_setup():
        import jax, jax.numpy as jnp
        import numpy as np
        NEG_INF = -9000000000000000.0
        ALPHA = 0.2
        H, F = (16, 64)
        key = jax.random.key(seed)
        k1, k2, k3, k4, k5 = jax.random.split(key, 5)
        B, N, D = (8, 512, 1024)
        h = jax.random.normal(k1, (B, N, D), dtype=jnp.float32)
        adj = jax.random.randint(k2, (B, N, N), 0, 2, dtype=jnp.int32)
        adj_weight = jax.random.uniform(k3, (B, N, N), dtype=jnp.float32)
        W = jax.random.normal(k4, (1, D, D), dtype=jnp.float32) * (1.414 * (6.0 / (2 * D)) ** 0.5)
        a = jax.random.normal(k5, (1, H, 2 * F, 1), dtype=jnp.float32) * 0.1
        return {'h': h, 'adj': adj, 'adj_weight': adj_weight, 'W': W, 'a': a}
    _L0_gnn_all = _L0_gnn_setup()
    _L0_gnn_in = {k: v for k, v in _L0_gnn_all.items() if k in ('W', 'a', )}
    del _L0_gnn_all

    return {
        "x": x,
        "adj": adj,
        "L0_gnn_W": _L0_gnn_in["W"],
        "L0_gnn_a": _L0_gnn_in["a"],
    }

def reference(x, adj, L0_gnn_W, L0_gnn_a):
    import jax
    import jax.numpy as jnp
    def _L0_gnn_ref(h, adj, adj_weight, W, a):
        import jax, jax.numpy as jnp
        import numpy as np
        NEG_INF = -9000000000000000.0
        ALPHA = 0.2
        H, F = (16, 64)
        B, N, D = h.shape
        Wh = jnp.matmul(h, W)
        Wh = Wh.reshape(B, N, H, F).transpose(0, 2, 1, 3)
        Wh1 = jnp.matmul(Wh, a[:, :, :F, :])
        Wh2 = jnp.matmul(Wh, a[:, :, F:, :])
        e = jax.nn.leaky_relu(Wh1 + Wh2, negative_slope=ALPHA)
        mask = (adj == 0)[:, None, :, :]
        att = jnp.where(mask, NEG_INF, e)
        att = jax.nn.softmax(att, axis=-1)
        att = att * adj_weight[:, None, :, :]
        h_prime = jnp.matmul(att, Wh)
        h_prime = h_prime.transpose(0, 2, 1, 3).reshape(B, N, H * F)
        return jax.nn.elu(h_prime)

    h = jnp.maximum(_layernorm(x, axis=-1), 0.0)
    x = x + _L0_gnn_ref(h, adj, adj, L0_gnn_W, L0_gnn_a)
    return x


_drawn_inputs = setup_inputs


def setup_inputs(seed=0):
    import zlib

    import numpy as np

    out = dict(_drawn_inputs(seed))
    spreads = {}
    factors = {}
    for name, (base, spread) in spreads.items():
        noise = np.random.default_rng([zlib.crc32(name.encode()), seed]).standard_normal(out[name].shape)
        drawn = base * np.exp(spread * noise) if base else spread * noise
        out[name] = jnp.asarray(drawn.astype(out[name].dtype))
    for name, factor in factors.items():
        out[name] = (out[name] * factor).astype(out[name].dtype)
    return out
```

```python
import concourse.bass as bass
from concourse import mybir
from contextlib import ExitStack

ALU = mybir.AluOpType
ACT = mybir.ActivationFunctionType
AX = mybir.AxisListType
F32 = mybir.dt.float32
F16 = mybir.dt.float16
BF16 = mybir.dt.bfloat16
I32 = mybir.dt.int32

P = 128
BANK = 512
UNROLL = 8
NEG_INF = -9000000000000000.0
ALPHA = 0.2
LN_EPS = 1e-5
H_SCALE = 1024.0
CAP_SLOPE = 6e35
NO_FLOOR = -3e38
LIMIT_OPS = 5
SCORE_OPS = 3
DENOM_OPS = 3


def gat_layer_kernel(nc, x, adj, w, a, out):
    B, N, D = x.shape
    _, H, F2, _ = a.shape
    F = F2 // 2
    KC = D // P
    JC = N // P
    HALVES = D // BANK
    TILES = B * JC
    FIRST, LAST = -2, TILES + 4
    LOOP_FROM = 5 + UNROLL
    TRIPS = (TILES - 2 - LOOP_FROM) // UNROLL
    LOOP_END = LOOP_FROM + TRIPS * UNROLL
    assert N % P == 0 and HALVES == 2 and H * F == D and UNROLL % (2 * JC) == 0 and TRIPS >= 1

    x_tiles = x.rearrange("b (t p) d -> (b t) p d", p=P)
    adj_tiles = adj.rearrange("b (t p) j -> (b t) p j", p=P)
    out_tiles = out.rearrange("b (t p) d -> (b t) p d", p=P)
    w_chunks = w.rearrange("o (c p) n -> (o c) p n", p=P)
    a_row = a.rearrange("o h f u -> (o u) (h f)")

    with ExitStack() as ctx:
        def sb(name, shape, dt):
            return ctx.enter_context(nc.sbuf_tensor(name, shape, dt))

        def ps(name, shape, dt):
            return ctx.enter_context(nc.psum_tensor(name, shape, dt))

        def sem(name):
            return ctx.enter_context(nc.semaphore(name))

        x_ring = sb("x_ring", [P, 8, D], F32)
        adj_ring = sb("adj_ring", [P, 4, N], I32)
        w_hi = sb("w_hi", [P, KC, D], F16)
        w_lo = sb("w_lo", [P, KC, D], F16)
        wh = sb("wh", [P, 2, 2, JC, D], F16)
        w_stage = wh[:].bitcast(F32).rearrange("p a b c d -> p (a b c d)").rearrange(
            "p (c n) -> p c n", c=KC)
        y = sb("y", [P, D], F32)
        h_hi = sb("h_hi", [P, 2, D], F16)
        h_lo = sb("h_lo", [P, 2, D], F16)
        hT = sb("hT", [P, 2, 2, KC, P], F16)
        adj_b = sb("adj_b", [P, 2, N], BF16)
        adj_mask = sb("adj_mask", [P, N], BF16)
        adjT = sb("adjT", [P, 2, JC, P], BF16)
        a_sb = sb("a_sb", [P, H * F2], F32)
        a_sum = sb("a_sum", [P, H, F], F32)
        prod = sb("prod", [P, H, F], F32)
        z = sb("z", [P, 2, H, F], F32)
        g = sb("g", [P, 2, D], F32)
        r = sb("r", [P, 2, D], F32)
        out_sb = sb("out_sb", [P, 2, D], F32)
        ident_h = sb("ident_h", [P, P], F16)
        ident_b = sb("ident_b", [P, P], BF16)
        half_neg = sb("half_neg", [P, 1], F32)
        stats = sb("stats", [P, 2, HALVES, 6], F32)
        mv = sb("mv", [P, 2, 2], F32)
        eps_col = sb("eps_col", [P, 1], F32)
        h_scale_col = sb("h_scale_col", [P, 1], F32)
        n_col = sb("n_col", [P, 1], F32)
        neg_row = sb("neg_row", [P, H], F32)
        var_eps = sb("var_eps", [P, 2], F32)
        root = sb("root", [P, 2], F32)
        rstd = sb("rstd", [P, 2], F32)
        cnt = sb("cnt", [P, 4], F32)
        e_raw = sb("e_raw", [P, H], F32)
        e_lr = sb("e_lr", [P, 4, H], F32)
        cap = sb("cap", [P, 1], F32)
        floor0 = sb("floor0", [P, 1], F32)
        floor = sb("floor", [P, 1], F32)
        e_cap = sb("e_cap", [P, 2, H], F32)
        e_max = sb("e_max", [P, 2, H], F32)
        diff = sb("diff", [P, 2, 2, H], F32)
        probs = sb("probs", [P, 2, 2, H], F32)
        rest = sb("rest", [P, 2], F32)
        den_in = sb("den_in", [P, H], F32)
        den_out = sb("den_out", [P, H], F32)
        den = sb("den", [P, 2, H], F32)
        rden = sb("rden", [P, H], F32)
        factor = sb("factor", [P, 2, H], F32)
        w_max = sb("w_max", [P, KC], F32)
        w_max1 = sb("w_max1", [P, 1], F32)
        w_maxall = sb("w_maxall", [P, 1], F32)
        w_pow = sb("w_pow", [P, 1], F32)
        w_powc = sb("w_powc", [P, 1], F32)
        w_rec = sb("w_rec", [P, 1], F32)
        w_scale = sb("w_scale", [P, 1], F32)
        w_inv = sb("w_inv", [P, 1], F32)

        acc = ps("acc", [P, 2, HALVES, BANK], F32)
        agg = ps("agg", [P, HALVES, BANK], F32)
        turn_a = ps("turn_a", [P, KC, P], F16)
        turn_b = ps("turn_b", [P, KC, P], F16)
        turn_adj = turn_a[:, 0:JC, :].bitcast(BF16)

        x_loaded = [sem(f"x_loaded{i}") for i in range(8)]
        adj_loaded = [sem(f"adj_loaded{i}") for i in range(4)]
        w_loaded = [sem(f"w_loaded{i}") for i in range(KC)]
        a_loaded = sem("a_loaded")
        stored = [sem(f"stored{i}") for i in range(2)]
        consts_zeroed = sem("consts_zeroed")
        consts_ready = sem("consts_ready")
        cols_ready = sem("cols_ready")
        w_stat = sem("w_stat")
        w_max_ready = sem("w_max_ready")
        w_maxall_ready = sem("w_maxall_ready")
        w_scale_ready = sem("w_scale_ready")
        w_hi_ready = sem("w_hi_ready")
        w_lo_ready = sem("w_lo_ready")
        a_added = sem("a_added")
        a_ready = sem("a_ready")
        stats_ready = sem("stats_ready")
        mv_ready = sem("mv_ready")
        norm_step = sem("norm_step")
        rstd_ready = sem("rstd_ready")
        y_ready = sem("y_ready")
        h_hi_ready = sem("h_hi_ready")
        h_lo_ready = sem("h_lo_ready")
        h_turned = sem("h_turned")
        hT_ready = sem("hT_ready")
        acc_ready = sem("acc_ready")
        wh_hi_ready = sem("wh_hi_ready")
        wh_lo_ready = sem("wh_lo_ready")
        prod_ready = sem("prod_ready")
        e_raw_ready = sem("e_raw_ready")
        e_ready = sem("e_ready")
        adj_ready = sem("adj_ready")
        cnt_ready = sem("cnt_ready")
        adj_turned = sem("adj_turned")
        adjT_ready = sem("adjT_ready")
        score_step = sem("score_step")
        limit_step = sem("limit_step")
        probs_ready = sem("probs_ready")
        denom_step = sem("denom_step")
        rden_ready = sem("rden_ready")
        factor_ready = sem("factor_ready")
        agg_ready = sem("agg_ready")
        z_ready = sem("z_ready")
        g_neg_ready = sem("g_neg_ready")
        g_exp_ready = sem("g_exp_ready")
        x_used = sem("x_used")
        out_ready = sem("out_ready")

        block = ctx.enter_context(nc.Block())

        def run_steps(eng, step):
            for k in range(FIRST, LOOP_FROM):
                step(0, k)
            with eng.Fori(0, TRIPS) as i:
                for k in range(LOOP_FROM, LOOP_FROM + UNROLL):
                    step(i, k)
            for k in range(LOOP_END, LAST + 1):
                step(0, k)

        def live(k):
            return 0 <= k < TILES

        def rank(i, k, ring=1):
            return (UNROLL // ring) * i + k // ring

        def tiles_done(i, k, each=1):
            return each * UNROLL * i + each * (k + 1)

        def wh_slot_free(eng, i, k):
            if k // JC >= 2:
                eng.wait_ge(agg_ready, UNROLL * i + JC * (k // JC) - JC)

        @block.sync
        def _(sp):
            def load_x(i, k):
                sp.dma_start(x_ring[:, k % 8, :], x_tiles[UNROLL * i + k]).then_inc(x_loaded[k % 8], 16)

            load_x(0, 0)
            load_x(0, 1)
            for c in range(KC):
                sp.dma_start(w_stage[:, c, :], w_chunks[c]).then_inc(w_loaded[c], 16)
            sp.dma_start(a_sb[:, :], a_row.to_broadcast([P, H * F2])).then_inc(a_loaded, 16)
            load_x(0, 2)

            def step(i, k):
                if live(k - 5) and live(k + 3):
                    sp.wait_ge(x_used, tiles_done(i, k - 5))
                if k + 3 >= 3 and live(k + 3):
                    load_x(i, k + 3)
                if live(k):
                    if k >= 4:
                        sp.wait_ge(cnt_ready, tiles_done(i, k - 4))
                    sp.dma_start(adj_ring[:, k % 4, :], adj_tiles[UNROLL * i + k]).then_inc(
                        adj_loaded[k % 4], 16)
                if live(k - 5):
                    sp.wait_ge(out_ready, tiles_done(i, k - 5))
                    sp.dma_start(out_tiles[UNROLL * i + k - 5], out_sb[:, (k - 5) % 2, :]).then_inc(
                        stored[(k - 5) % 2], 16)

            run_steps(sp, step)
            for slot in range(2):
                sp.wait_ge(stored[slot], 16 * (TILES // 2))

        @block.gpsimd
        def _(pool):
            for col, value in ((half_neg, -0.5), (eps_col, LN_EPS), (h_scale_col, H_SCALE), (n_col, float(N)),
                               (neg_row, NEG_INF)):
                pool.memset(col[:, :], value).then_inc(cols_ready, 1)
            pool.wait_ge(cols_ready, 5)
            for m in (ident_h, ident_b):
                pool.memset(m[:, :], 0.0).then_inc(consts_zeroed, 1)
            pool.wait_ge(consts_zeroed, 2)
            for m in (ident_h, ident_b):
                pool.affine_select(out=m[:, :], in_=m[:, :], compare_op=ALU.not_equal, fill=1.0, base=0,
                                   pattern=[[-1, P]], channel_multiplier=1).then_inc(consts_ready, 1)

            def layer_norm_scale(i, k):
                slot = slice(k % 2, k % 2 + 1)
                pool.wait_ge(mv_ready, tiles_done(i, k))
                pool.tensor_tensor(var_eps[:, slot], mv[:, k % 2, 1:2], eps_col[:, :], ALU.add).then_inc(
                    norm_step, 1)
                pool.wait_ge(norm_step, tiles_done(i, k, 2) - 1)
                pool.tensor_tensor(root[:, slot], var_eps[:, slot], half_neg[:, :], ALU.pow).then_inc(norm_step, 1)
                if k >= 2:
                    pool.wait_ge(y_ready, tiles_done(i, k - 2))
                pool.wait_ge(norm_step, tiles_done(i, k, 2))
                pool.tensor_tensor(rstd[:, slot], root[:, slot], h_scale_col[:, :], ALU.mult).then_inc(
                    rstd_ready, 1)

            def scores(i, k):
                slot = k % 2
                c = cnt[:, k % 4:k % 4 + 1]

                if k >= 2:
                    pool.wait_ge(probs_ready, tiles_done(i, k - 2))
                    pool.wait_ge(denom_step, tiles_done(i, k - 2, DENOM_OPS))
                pool.wait_ge(limit_step, tiles_done(i, k, LIMIT_OPS))
                pool.tensor_tensor(diff[:, slot, 0, :], e_cap[:, slot, :], e_max[:, slot, :],
                                   ALU.subtract).then_inc(score_step, 1)
                pool.tensor_tensor(diff[:, slot, 1, :], neg_row[:, :], e_max[:, slot, :],
                                   ALU.subtract).then_inc(score_step, 1)
                pool.tensor_tensor(rest[:, slot:slot + 1], n_col[:, :], c, ALU.subtract).then_inc(score_step, 1)

            def denominators(i, k):
                slot = k % 2
                c = cnt[:, k % 4:k % 4 + 1]

                if k >= 2:
                    pool.wait_ge(rden_ready, tiles_done(i, k - 2))
                pool.wait_ge(probs_ready, tiles_done(i, k))
                pool.tensor_tensor(den_in[:, :], probs[:, slot, 0, :], c.to_broadcast([P, H]), ALU.mult).then_inc(
                    denom_step, 1)
                pool.tensor_tensor(den_out[:, :], probs[:, slot, 1, :],
                                   rest[:, slot:slot + 1].to_broadcast([P, H]), ALU.mult).then_inc(denom_step, 1)
                pool.wait_ge(denom_step, DENOM_OPS * UNROLL * i + DENOM_OPS * k + 2)
                pool.tensor_tensor(den[:, slot, :], den_in[:, :], den_out[:, :], ALU.add).then_inc(denom_step, 1)

            def step(i, k):
                if live(k + 2):
                    layer_norm_scale(i, k + 2)
                if k == -1:
                    pool.wait_ge(w_max_ready, 1)
                    pool.partition_all_reduce(w_maxall[:, :], w_max1[:, :], P,
                                              bass.bass_isa.ReduceOp.max).then_inc(w_maxall_ready, 1)
                if live(k - 4):
                    denominators(i, k - 4)
                if live(k - 3):
                    scores(i, k - 3)

            run_steps(pool, step)

        @block.scalar
        def _(act):
            def split_w_hi():
                act.wait_ge(w_scale_ready, 1)
                for c in range(KC):
                    act.activation(w_hi[:, c, :], w_stage[:, c, :], ACT.Copy,
                                   scale=w_scale[:, :]).then_inc(w_hi_ready, 1)

            def copy_hT(i, k):
                for part, turn in enumerate((turn_a, turn_b)):
                    act.wait_ge(h_turned, tiles_done(i, k, 2) - 1 + part)
                    if k >= 2:
                        act.wait_ge(acc_ready, tiles_done(i, k - 2))
                    act.activation(hT[:, k % 2, part, :, :], turn[:, :, :], ACT.Copy).then_inc(hT_ready, 1)

            def elu_exp(i, k):
                act.wait_ge(z_ready, tiles_done(i, k))
                if k >= 2:
                    act.wait_ge(out_ready, tiles_done(i, k - 2))
                act.activation(g[:, k % 2, :], z[:, k % 2, :, :], ACT.Relu, scale=-1.0).then_inc(
                    g_neg_ready, 1)
                act.wait_ge(g_neg_ready, tiles_done(i, k))
                act.activation(g[:, k % 2, :], g[:, k % 2, :], ACT.Exp, scale=-1.0).then_inc(g_exp_ready, 1)

            def relu_hi(i, k):
                act.wait_ge(y_ready, tiles_done(i, k))
                if k >= 2:
                    act.wait_ge(h_turned, tiles_done(i, k - 2, 2))
                act.activation(h_hi[:, k % 2, :], y[:, :], ACT.Relu).then_inc(h_hi_ready, 1)

            def copy_adjT(i, k):
                act.wait_ge(adj_turned, tiles_done(i, k))
                if k >= 2:
                    act.wait_ge(agg_ready, tiles_done(i, k - 2))
                act.activation(adjT[:, k % 2, :, :], turn_adj, ACT.Copy).then_inc(adjT_ready, 1)

            def softmax_exp(i, k):
                act.wait_ge(score_step, tiles_done(i, k, SCORE_OPS))
                if k >= 2:
                    act.wait_ge(factor_ready, tiles_done(i, k - 2))
                act.activation(probs[:, k % 2, :, :], diff[:, k % 2, :, :], ACT.Exp).then_inc(probs_ready, 1)

            def wh_hi(i, k):
                act.wait_ge(acc_ready, tiles_done(i, k))
                wh_slot_free(act, i, k)
                for half in range(HALVES):
                    act.activation(wh[:, k // JC % 2, 0, k % JC, half * BANK:(half + 1) * BANK],
                                   acc[:, k % 2, half, :], ACT.Copy,
                                   scale=1.0 / H_SCALE).then_inc(wh_hi_ready, 1)

            def step(i, k):
                if live(k + 1):
                    copy_hT(i, k + 1)
                if live(k - 5):
                    elu_exp(i, k - 5)
                if live(k + 2):
                    relu_hi(i, k + 2)
                if k == -1:
                    split_w_hi()
                if live(k - 3):
                    copy_adjT(i, k - 3)
                    softmax_exp(i, k - 3)
                if live(k):
                    wh_hi(i, k)

            run_steps(act, step)

        @block.vector
        def _(dve):
            def w_scale_steps():
                for c in range(KC):
                    dve.wait_ge(w_loaded[c], 16)
                    dve.tensor_reduce(out=w_max[:, c:c + 1], in_=w_stage[:, c, :], axis=AX.X, op=ALU.max,
                                      apply_absolute_value=True).then_inc(w_stat, 1)
                dve.wait_ge(w_stat, KC)
                dve.tensor_reduce(out=w_max1[:, :], in_=w_max[:, :], axis=AX.X, op=ALU.max).then_inc(
                    w_max_ready, 1)
                dve.wait_ge(a_loaded, 16)
                a_heads = a_sb[:, :].rearrange("p (h f) -> p h f", h=H)
                dve.tensor_tensor(a_sum[:, :, :], a_heads[:, :, 0:F], a_heads[:, :, F:F2], ALU.add).then_inc(
                    a_added, 1)
                dve.wait_ge(w_maxall_ready, 1)
                dve.tensor_scalar(w_pow[:, :].bitcast(I32), w_maxall[:, :].bitcast(I32), 0x7F800000, None,
                                  ALU.bitwise_and).then_inc(w_stat, 1)
                dve.wait_ge(w_stat, KC + 1)
                dve.tensor_scalar(w_powc[:, :], w_pow[:, :], 2.0 ** -110, 2.0 ** 126, ALU.max,
                                  ALU.min).then_inc(w_stat, 1)
                dve.wait_ge(w_stat, KC + 2)
                dve.reciprocal(w_rec[:, :], w_powc[:, :]).then_inc(w_stat, 1)
                dve.wait_ge(w_stat, KC + 3)
                dve.tensor_scalar(w_scale[:, :], w_rec[:, :], 16.0, None, ALU.mult).then_inc(w_scale_ready, 1)
                dve.tensor_scalar(w_inv[:, :], w_powc[:, :], 1.0 / 16.0, None, ALU.mult).then_inc(w_stat, 1)
                dve.wait_ge(w_scale_ready, 1)
                for c in range(KC):
                    dve.wait_ge(w_hi_ready, c + 1)
                    dve.scalar_tensor_tensor(out=w_lo[:, c, :], in0=w_stage[:, c, :], scalar=w_scale[:, :],
                                             in1=w_hi[:, c, :], op0=ALU.mult, op1=ALU.subtract).then_inc(
                        w_lo_ready, 1)
                dve.wait_ge(w_stat, KC + 4)
                dve.wait_ge(a_added, 1)
                dve.tensor_scalar(a_sum[:, :, :], a_sum[:, :, :], w_inv[:, :], 1.0 / H_SCALE, ALU.mult,
                                  ALU.mult).then_inc(a_ready, 1)

            def wh_lo(i, k):
                wh_slot_free(dve, i, k)
                for half in range(HALVES):
                    cols = slice(half * BANK, (half + 1) * BANK)
                    dve.wait_ge(wh_hi_ready, tiles_done(i, k, 2) - 1 + half)
                    dve.scalar_tensor_tensor(out=wh[:, k // JC % 2, 1, k % JC, cols], in0=acc[:, k % 2, half, :],
                                             scalar=1.0 / H_SCALE, in1=wh[:, k // JC % 2, 0, k % JC, cols],
                                             op0=ALU.mult, op1=ALU.subtract).then_inc(wh_lo_ready, 1)

            def score_products(i, k):
                if k == 0:
                    dve.wait_ge(a_ready, 1)
                acc_heads = acc[:, k % 2, :, :].rearrange("p a (h f) -> p (a h) f", f=F)
                dve.tensor_tensor(prod[:, :, :], acc_heads, a_sum[:, :, :], ALU.mult).then_inc(prod_ready, 1)

            def score_sums(i, k):
                dve.wait_ge(prod_ready, tiles_done(i, k))
                dve.tensor_reduce(out=e_raw[:, :], in_=prod[:, :, :], axis=AX.X, op=ALU.add).then_inc(
                    e_raw_ready, 1)

            def leaky_relu(i, k):
                dve.wait_ge(e_raw_ready, tiles_done(i, k))
                dve.scalar_tensor_tensor(out=e_lr[:, k % 4, :], in0=e_raw[:, :], scalar=ALPHA, in1=e_raw[:, :],
                                         op0=ALU.mult, op1=ALU.max).then_inc(e_ready, 1)

            def scale_rows(i, k):
                dve.wait_ge(agg_ready, tiles_done(i, k))
                dve.wait_ge(factor_ready, tiles_done(i, k))
                if k >= 2:
                    dve.wait_ge(g_neg_ready, tiles_done(i, k - 2))
                agg_heads = agg[:, :, :].rearrange("p a (h f) -> p (a h) f", f=F)
                row_factor = factor[:, k % 2, :].unsqueeze(2).to_broadcast([P, H, F])
                dve.tensor_tensor(z[:, k % 2, :, :], agg_heads, row_factor, ALU.mult).then_inc(z_ready, 1)

            def add_positive(i, k):
                dve.wait_ge(z_ready, tiles_done(i, k))
                z_row = z[:, k % 2, :, :].rearrange("p h f -> p (h f)")
                dve.scalar_tensor_tensor(out=r[:, k % 2, :], in0=z_row, scalar=0.0, in1=x_ring[:, k % 8, :],
                                         op0=ALU.max, op1=ALU.add).then_inc(x_used, 1)

            def add_negative(i, k):
                dve.wait_ge(g_exp_ready, tiles_done(i, k))
                dve.wait_ge(x_used, tiles_done(i, k))
                if k >= 2:
                    dve.wait_ge(stored[k % 2], 16 * rank(i, k, 2))
                dve.scalar_tensor_tensor(out=out_sb[:, k % 2, :], in0=g[:, k % 2, :], scalar=-1.0,
                                         in1=r[:, k % 2, :], op0=ALU.add, op1=ALU.add).then_inc(out_ready, 1)

            def row_stats(i, k):
                dve.wait_ge(x_loaded[k % 8], 16 * rank(i, k, 8) + 16)
                for half in range(HALVES):
                    dve.bn_stats(stats[:, k % 2, half, :],
                                 x_ring[:, k % 8, half * BANK:(half + 1) * BANK]).then_inc(stats_ready, 1)

            def row_moments(i, k):
                dve.bn_aggr(mv[:, k % 2, :], stats[:, k % 2, :, :].rearrange("p a b -> p (a b)")).then_inc(
                    mv_ready, 1)

            def normalise(i, k):
                dve.wait_ge(rstd_ready, tiles_done(i, k))
                dve.wait_ge(mv_ready, tiles_done(i, k))
                if k >= 1:
                    dve.wait_ge(h_lo_ready, tiles_done(i, k - 1))
                dve.tensor_scalar(y[:, :], x_ring[:, k % 8, :], mv[:, k % 2, 0:1], rstd[:, k % 2:k % 2 + 1],
                                  ALU.subtract, ALU.mult).then_inc(y_ready, 1)

            def relu_lo(i, k):
                dve.wait_ge(h_hi_ready, tiles_done(i, k))
                if k >= 2:
                    dve.wait_ge(h_turned, tiles_done(i, k - 2, 2))
                dve.scalar_tensor_tensor(out=h_lo[:, k % 2, :], in0=y[:, :], scalar=0.0, in1=h_hi[:, k % 2, :],
                                         op0=ALU.max, op1=ALU.subtract).then_inc(h_lo_ready, 1)

            def convert_adj(i, k):
                dve.wait_ge(adj_loaded[k % 4], 16 * rank(i, k, 4) + 16)
                if k >= 2:
                    dve.wait_ge(adj_turned, tiles_done(i, k - 2))
                dve.tensor_copy(adj_b[:, k % 2, :], adj_ring[:, k % 4, :]).then_inc(adj_ready, 1)

            def count_neighbours(i, k):
                dve.wait_ge(adj_ready, tiles_done(i, k))
                if k >= 4:
                    dve.wait_ge(denom_step, tiles_done(i, k - 4, DENOM_OPS))
                dve.tensor_scalar(adj_mask[:, :], adj_b[:, k % 2, :], 0.0, 0.0, ALU.not_equal, ALU.add,
                                  accum_out=cnt[:, k % 4:k % 4 + 1]).then_inc(cnt_ready, 1)

            def row_limits(i, k):
                c = cnt[:, k % 4:k % 4 + 1]

                def limit_done(j):
                    dve.wait_ge(limit_step, LIMIT_OPS * UNROLL * i + LIMIT_OPS * k + j)

                dve.wait_ge(cnt_ready, tiles_done(i, k))
                dve.tensor_scalar(cap[:, :], c, CAP_SLOPE, NEG_INF, ALU.mult, ALU.add).then_inc(limit_step, 1)
                dve.tensor_scalar(floor0[:, :], c, float(N), NO_FLOOR, ALU.is_ge, ALU.mult).then_inc(limit_step, 1)
                limit_done(2)
                dve.tensor_scalar(floor[:, :], floor0[:, :], NEG_INF, None, ALU.min).then_inc(limit_step, 1)
                dve.wait_ge(e_ready, tiles_done(i, k))
                if k >= 2:
                    dve.wait_ge(score_step, tiles_done(i, k - 2, SCORE_OPS))
                dve.tensor_scalar(e_cap[:, k % 2, :], e_lr[:, k % 4, :], cap[:, :], None, ALU.min).then_inc(
                    limit_step, 1)
                limit_done(3)
                dve.tensor_scalar(e_max[:, k % 2, :], e_lr[:, k % 4, :], cap[:, :], floor[:, :], ALU.min,
                                  ALU.max).then_inc(limit_step, 1)

            def invert_denominator(i, k):
                dve.wait_ge(denom_step, tiles_done(i, k, DENOM_OPS))
                dve.reciprocal(rden[:, :], den[:, k % 2, :]).then_inc(rden_ready, 1)

            def row_factors(i, k):
                dve.wait_ge(rden_ready, tiles_done(i, k))
                if k >= 1:
                    dve.wait_ge(z_ready, tiles_done(i, k - 1))
                dve.scalar_tensor_tensor(out=factor[:, k % 2, :], in0=rden[:, :], scalar=w_inv[:, :],
                                         in1=probs[:, k % 2, 0, :], op0=ALU.mult, op1=ALU.mult).then_inc(
                    factor_ready, 1)

            def step(i, k):
                if live(k - 1):
                    wh_lo(i, k - 1)
                if live(k - 5):
                    scale_rows(i, k - 5)
                if live(k - 1):
                    score_products(i, k - 1)
                if live(k - 5):
                    add_positive(i, k - 5)
                if live(k + 2):
                    row_stats(i, k + 2)
                if live(k + 2):
                    dve.wait_ge(stats_ready, tiles_done(i, k + 2, 2))
                if live(k - 1):
                    score_sums(i, k - 1)
                if live(k + 2):
                    row_moments(i, k + 2)
                if live(k - 4):
                    invert_denominator(i, k - 4)
                if live(k + 2):
                    normalise(i, k + 2)
                if live(k - 1):
                    leaky_relu(i, k - 1)
                if live(k - 4):
                    row_factors(i, k - 4)
                if live(k - 2):
                    convert_adj(i, k - 2)
                if live(k - 3):
                    row_limits(i, k - 3)
                if live(k - 5):
                    add_negative(i, k - 5)
                if live(k - 2):
                    count_neighbours(i, k - 2)
                if live(k + 2):
                    relu_lo(i, k + 2)
                if k == -1:
                    w_scale_steps()

            run_steps(dve, step)

        @block.tensor
        def _(pe):
            def turn_h(i, k):
                if k >= 1:
                    pe.wait_ge(hT_ready, tiles_done(i, k - 1, 2))
                if k == 0:
                    pe.wait_ge(consts_ready, 2)
                if k >= 5:
                    pe.wait_ge(adjT_ready, tiles_done(i, k - 5))
                for src, ready, turn in ((h_hi, h_hi_ready, turn_a), (h_lo, h_lo_ready, turn_b)):
                    pe.wait_ge(ready, tiles_done(i, k))
                    for c in range(KC):
                        last = pe.transpose(turn[:, c, :], src[:, k % 2, c * P:(c + 1) * P], ident_h[:, :])
                    last.then_inc(h_turned, 1)

            def project(i, k):
                pe.wait_ge(hT_ready, tiles_done(i, k, 2))
                if k >= 2:
                    pe.wait_ge(prod_ready, tiles_done(i, k - 2))
                for c in range(KC):
                    if k == 0:
                        pe.wait_ge(w_hi_ready, c + 1)
                        pe.wait_ge(w_lo_ready, c + 1)
                    for h_part, w_part in ((0, w_hi), (0, w_lo), (1, w_hi)):
                        for half in range(HALVES):
                            last = pe.matmul(acc[:, k % 2, half, :], hT[:, k % 2, h_part, c, :],
                                             w_part[:, c, half * BANK:(half + 1) * BANK],
                                             start=(c == 0 and h_part == 0 and w_part is w_hi),
                                             stop=(c == KC - 1 and h_part == 1))
                last.then_inc(acc_ready, 1)

            def turn_adj_tile(i, k):
                pe.wait_ge(adj_ready, tiles_done(i, k))
                if live(k + 4):
                    pe.wait_ge(hT_ready, tiles_done(i, k + 4, 2))
                elif k >= 1:
                    pe.wait_ge(adjT_ready, tiles_done(i, k - 1))
                for c in range(JC):
                    last = pe.transpose(turn_adj[:, c, :], adj_b[:, k % 2, c * P:(c + 1) * P], ident_b[:, :])
                last.then_inc(adj_turned, 1)

            def aggregate(i, k):
                pe.wait_ge(adjT_ready, tiles_done(i, k))
                pe.wait_ge(wh_lo_ready, 2 * UNROLL * i + 2 * JC * (k // JC + 1))
                if k >= 1:
                    pe.wait_ge(z_ready, tiles_done(i, k - 1))
                for c in range(JC):
                    for part in range(2):
                        for half in range(HALVES):
                            last = pe.matmul(agg[:, half, :], adjT[:, k % 2, c, :],
                                             wh[:, k // JC % 2, part, c, half * BANK:(half + 1) * BANK],
                                             start=(c == 0 and part == 0), stop=(c == JC - 1 and part == 1))
                last.then_inc(agg_ready, 1)

            def step(i, k):
                if live(k + 1):
                    turn_h(i, k + 1)
                if live(k):
                    project(i, k)
                if live(k - 3):
                    turn_adj_tile(i, k - 3)
                if live(k - 4):
                    aggregate(i, k - 4)

            run_steps(pe, step)


_INS = ["x", "adj", "L0_gnn_W", "L0_gnn_a"]


def kernel(**inputs):
    import numpy as _np
    import concourse.bacc as _bacc
    from concourse import mybir as _mybir
    from concourse.bass_utils import run_bass_kernel_spmd as _run

    nc = _bacc.Bacc("TRN2", target_bir_lowering=False, num_devices=1)
    arrays, args = {}, []
    for name in _INS:
        arr = _np.ascontiguousarray(inputs[name])
        arrays[f"in_{name}"] = arr
        args.append(nc.dram_tensor(f"in_{name}", arr.shape, _mybir.dt.from_np(arr.dtype),
                                   kind="ExternalInput").ap())
    shape = _np.shape(inputs["x"])
    args.append(nc.dram_tensor("out", shape, _mybir.dt.float32, kind="ExternalOutput").ap())
    gat_layer_kernel(nc, *args)
    result = _run(nc, [arrays], core_ids=[0])
    return result.results[0]["out"]
```

```python
import concourse.bass as bass
from concourse import mybir
from contextlib import ExitStack

ALU = mybir.AluOpType
ACT = mybir.ActivationFunctionType
AX = mybir.AxisListType
F32 = mybir.dt.float32
F16 = mybir.dt.float16
BF16 = mybir.dt.bfloat16
I32 = mybir.dt.int32

P = 128
W_EARLY = (0, 2, 5)
BANK = 512
UNROLL = 8
NEG_INF = -9000000000000000.0
ALPHA = 0.2
LN_EPS = 1e-5
H_SCALE = 1024.0
CAP_SLOPE = 6e35
NO_FLOOR = -3e38
ADJ_PARTS = 3
EXACT_SQUARES = 65536.0
NORM_OPS = 3
LIMIT_OPS = 4
SCORE_OPS = 2
DENOM_OPS = 3


def gat_layer_kernel(nc, x, adj, w, a, out):
    B, N, D = x.shape
    _, H, F2, _ = a.shape
    F = F2 // 2
    KC = D // P
    JC = N // P
    HALVES = D // BANK
    TILES = B * JC
    FIRST, LAST = -2, TILES + 5
    LOOP_FROM = 5 + UNROLL
    TRIPS = (TILES - 3 - LOOP_FROM) // UNROLL
    LOOP_END = LOOP_FROM + TRIPS * UNROLL
    assert N % P == 0 and HALVES == 2 and H * F == D and UNROLL % (2 * JC) == 0 and TRIPS >= 1

    x_tiles = x.rearrange("b (t p) d -> (b t) p d", p=P)
    adj_tiles = adj.rearrange("b (t p) j -> (b t) p j", p=P)
    out_tiles = out.rearrange("b (t p) d -> (b t) p d", p=P)
    w_chunks = w.rearrange("o (c p) n -> (o c) p n", p=P)
    a_row = a.rearrange("o h f u -> (o u) (h f)")

    with ExitStack() as ctx:
        def sb(name, shape, dt):
            return ctx.enter_context(nc.sbuf_tensor(name, shape, dt))

        def ps(name, shape, dt):
            return ctx.enter_context(nc.psum_tensor(name, shape, dt))

        def sem(name):
            return ctx.enter_context(nc.semaphore(name))

        x_ring = sb("x_ring", [P, 8, D], F32)
        adj_ring = sb("adj_ring", [P, 4, N], I32)
        w_hi = sb("w_hi", [P, KC, D], F16)
        w_lo = sb("w_lo", [P, KC, D], F16)
        wh = sb("wh", [P, 2, 2, JC, D], F16)
        w_stage = wh[:].bitcast(F32).rearrange("p a b c d -> p (a b c d)").rearrange(
            "p (c n) -> p c n", c=KC)
        y = sb("y", [P, 2, D], F32)
        h = sb("h", [P, 2, 2, D], F16)
        hT = sb("hT", [P, 2, 2, KC, P], F16)
        adj_b = sb("adj_b", [P, 2, ADJ_PARTS, N], BF16)
        adj_mask = sb("adj_mask", [P, N], BF16)
        adjT = sb("adjT", [P, 2, ADJ_PARTS, JC, P], BF16)
        adj_rest = sb("adj_rest", [P, N], F32)
        square = sb("square", [P, N], BF16)
        squares = sb("squares", [P, 4], F32)
        worst = sb("worst", [P, 1], F32)
        worst_all = sb("worst_all", [P, 1], F32)
        adj_flag = sb("adj_flag", [P, 1], I32)
        a_sb = sb("a_sb", [P, H * F2], F32)
        a_sum = sb("a_sum", [P, H, F], F32)
        prod = sb("prod", [P, H, F], F32)
        z = sb("z", [P, 2, H, F], F32)
        g = sb("g", [P, 2, D], F32)
        r = sb("r", [P, 2, D], F32)
        out_sb = sb("out_sb", [P, 2, D], F32)
        half_neg = sb("half_neg", [P, 1], F32)
        stats = sb("stats", [P, 2, HALVES, 6], F32)
        mv = sb("mv", [P, 2, 2], F32)
        eps_col = sb("eps_col", [P, 1], F32)
        h_scale_col = sb("h_scale_col", [P, 1], F32)
        n_col = sb("n_col", [P, 1], F32)
        neg_row = sb("neg_row", [P, H], F32)
        var_eps = sb("var_eps", [P, 2], F32)
        minus_col = sb("minus_col", [P, 1], F32)
        mean_neg = sb("mean_neg", [P, 2], F32)
        root = sb("root", [P, 2], F32)
        shift = sb("shift", [P, 2], F32)
        rstd = sb("rstd", [P, 2], F32)
        cnt = sb("cnt", [P, 4], F32)
        e_raw = sb("e_raw", [P, H], F32)
        e_lr = sb("e_lr", [P, 4, H], F32)
        cap = sb("cap", [P, 2], F32)
        floor0 = sb("floor0", [P, 2], F32)
        floor = sb("floor", [P, 2], F32)
        e_cap = sb("e_cap", [P, 2, H], F32)
        e_max = sb("e_max", [P, 2, H], F32)
        diff = sb("diff", [P, 2, 2, H], F32)
        probs = sb("probs", [P, 2, 2, H], F32)
        rest = sb("rest", [P, 4], F32)
        den_in = sb("den_in", [P, H], F32)
        den_out = sb("den_out", [P, H], F32)
        den = sb("den", [P, 2, H], F32)
        rden = sb("rden", [P, H], F32)
        factor = sb("factor", [P, 2, H], F32)
        w_max = sb("w_max", [P, KC], F32)
        w_max1 = sb("w_max1", [P, 1], F32)
        w_maxall = sb("w_maxall", [P, 1], F32)
        w_pow = sb("w_pow", [P, 1], F32)
        w_powc = sb("w_powc", [P, 1], F32)
        w_rec = sb("w_rec", [P, 1], F32)
        w_scale = sb("w_scale", [P, 1], F32)
        w_inv = sb("w_inv", [P, 1], F32)

        acc = ps("acc", [P, 2, HALVES, BANK], F32)
        agg = ps("agg", [P, 2, HALVES, BANK], F32)

        w_loaded = [sem(f"w_loaded{i}") for i in range(KC)]
        a_loaded = sem("a_loaded")
        cols_ready = sem("cols_ready")
        w_stat = sem("w_stat")
        w_max_ready = sem("w_max_ready")
        w_maxall_ready = sem("w_maxall_ready")
        w_scale_ready = sem("w_scale_ready")
        w_hi_ready = sem("w_hi_ready")
        w_lo_ready = sem("w_lo_ready")
        a_added = sem("a_added")
        a_ready = sem("a_ready")
        worst_zeroed = sem("worst_zeroed")
        worst_all_ready = sem("worst_all_ready")
        flag_ready = sem("flag_ready")
        all_stored = sem("all_stored")

        class Run:

            def __init__(self, tag, parts):
                self.parts = parts
                self.exact = parts > 1
                self.x_loaded = [sem(f"{tag}_x_loaded{i}") for i in range(8)]
                self.adj_loaded = [sem(f"{tag}_adj_loaded{i}") for i in range(4)]
                self.stored = [sem(f"{tag}_stored{i}") for i in range(2)]
                self.stats_ready = sem(f"{tag}_stats_ready")
                self.mv_ready = sem(f"{tag}_mv_ready")
                self.norm_step = sem(f"{tag}_norm_step")
                self.rstd_ready = sem(f"{tag}_rstd_ready")
                self.shift_ready = sem(f"{tag}_shift_ready")
                self.y_ready = sem(f"{tag}_y_ready")
                self.h_hi_ready = sem(f"{tag}_h_hi_ready")
                self.h_lo_ready = sem(f"{tag}_h_lo_ready")
                self.h_turned = [sem(f"{tag}_h_turned{i}") for i in range(2)]
                self.acc_ready = sem(f"{tag}_acc_ready")
                self.wh_hi_ready = sem(f"{tag}_wh_hi_ready")
                self.wh_lo_ready = sem(f"{tag}_wh_lo_ready")
                self.prod_ready = sem(f"{tag}_prod_ready")
                self.e_raw_ready = sem(f"{tag}_e_raw_ready")
                self.e_ready = sem(f"{tag}_e_ready")
                self.adj_ready = sem(f"{tag}_adj_ready")
                self.cnt_ready = sem(f"{tag}_cnt_ready")
                self.adj_turned = [sem(f"{tag}_adj_turned{i}") for i in range(2)]
                self.score_step = sem(f"{tag}_score_step")
                self.limit_step = sem(f"{tag}_limit_step")
                self.score_ready = sem(f"{tag}_score_ready")
                self.probs_ready = sem(f"{tag}_probs_ready")
                self.denom_step = sem(f"{tag}_denom_step")
                self.rden_ready = sem(f"{tag}_rden_ready")
                self.factor_ready = sem(f"{tag}_factor_ready")
                self.agg_ready = sem(f"{tag}_agg_ready")
                self.z_ready = sem(f"{tag}_z_ready")
                self.g_neg_ready = sem(f"{tag}_g_neg_ready")
                self.g_exp_ready = sem(f"{tag}_g_exp_ready")
                self.x_used = sem(f"{tag}_x_used")
                self.out_ready = sem(f"{tag}_out_ready")
                self.resid_ready = sem(f"{tag}_resid_ready")
                self.mid_ready = sem(f"{tag}_mid_ready")
                self.low_ready = sem(f"{tag}_low_ready")
                self.squares_ready = sem(f"{tag}_squares_ready")
                self.worst_ready = sem(f"{tag}_worst_ready")

        runs = (Run("fast", 1), Run("exact", ADJ_PARTS))

        block = ctx.enter_context(nc.Block())

        def run_steps(eng, step):
            for k in range(FIRST, LOOP_FROM):
                step(0, k)
            with eng.Fori(0, TRIPS) as i:
                for k in range(LOOP_FROM, LOOP_FROM + UNROLL):
                    step(i, k)
            for k in range(LOOP_END, LAST + 1):
                step(0, k)

        def live(k):
            return 0 <= k < TILES

        def rank(i, k, ring=1):
            return (UNROLL // ring) * i + k // ring

        def tiles_done(i, k, each=1):
            return each * UNROLL * i + each * (k + 1)

        def exact_run_if_needed(eng, over_tiles):
            eng.wait_ge(flag_ready, 1)
            flag = eng.value_load(adj_flag[0:1, 0:1], min_val=0, max_val=1)
            with eng.If(flag > 0):
                eng.wait_ge(all_stored, 1)
                over_tiles(runs[1])

        def wh_slot_free(eng, run, i, k):
            if k // JC >= 2:
                eng.wait_ge(run.agg_ready, UNROLL * i + JC * (k // JC) - JC)

        @block.sync
        def _(sp):
            def over_tiles(run):
                def load_x(i, k):
                    sp.dma_start(x_ring[:, k % 8, :], x_tiles[UNROLL * i + k]).then_inc(run.x_loaded[k % 8], 16)

                load_x(0, 0)
                load_x(0, 1)
                if not run.exact:
                    for c in range(KC):
                        sp.dma_start(w_stage[:, c, :], w_chunks[c]).then_inc(w_loaded[c], 16)
                    sp.dma_start(a_sb[:, :], a_row.to_broadcast([P, H * F2])).then_inc(a_loaded, 16)
                load_x(0, 2)

                def turn_h(i, k):
                    sp.dma_start_transpose(hT[:, k % 2, :, :, :].rearrange("p a c r -> p (a c) r"),
                                           h[:, k % 2, :, :].rearrange("p a d -> p (a d)")).then_inc(
                        run.h_turned[k % 2], 16)

                def turn_adj(i, k):
                    sp.dma_start_transpose(adjT[:, k % 2, 0:run.parts, :, :].rearrange("p a c r -> p (a c) r"),
                                           adj_b[:, k % 2, 0:run.parts, :].rearrange("p a j -> p (a j)")).then_inc(
                        run.adj_turned[k % 2], 16)

                def step(i, k):
                    counts = {back: tiles_done(i, k - back) for back in (-1, 1, 3, 4, 5, 6)}
                    if k in range(LOOP_FROM, LOOP_FROM + UNROLL):
                        for count in counts.values():
                            sp.compute_val(count)
                    if live(k + 1):
                        sp.wait_ge(run.h_hi_ready, counts[-1])
                        sp.wait_ge(run.h_lo_ready, counts[-1])
                        if k >= 1:
                            sp.wait_ge(run.acc_ready, counts[1])
                    if live(k - 3):
                        adj_done = run.low_ready if run.exact else run.adj_ready
                        sp.wait_ge(adj_done, counts[3])
                        if k >= 5:
                            sp.wait_ge(run.agg_ready, counts[5])
                    if live(k):
                        if k >= 4:
                            sp.wait_ge(run.resid_ready if run.exact else run.adj_ready, counts[4])
                        sp.dma_start(adj_ring[:, k % 4, :], adj_tiles[UNROLL * i + k]).then_inc(
                            run.adj_loaded[k % 4], 16)
                    if live(k + 1):
                        turn_h(i, k + 1)
                    if live(k - 3):
                        turn_adj(i, k - 3)
                    if live(k - 5) and live(k + 3):
                        sp.wait_ge(run.x_used, counts[5])
                    if k + 3 >= 3 and live(k + 3):
                        load_x(i, k + 3)
                    if live(k - 6):
                        sp.wait_ge(run.out_ready, counts[6])
                        sp.dma_start(out_tiles[UNROLL * i + k - 6], out_sb[:, k % 2, :]).then_inc(
                            run.stored[k % 2], 16)

                run_steps(sp, step)
                for slot in range(2):
                    sp.wait_ge(run.stored[slot], 16 * (TILES // 2))
                if not run.exact:
                    sp.sem_inc(all_stored, 1)

            over_tiles(runs[0])
            exact_run_if_needed(sp, over_tiles)

        @block.gpsimd
        def _(pool):
            for col, value in ((half_neg, -0.5), (eps_col, LN_EPS), (h_scale_col, H_SCALE), (n_col, float(N)),
                               (neg_row, NEG_INF), (minus_col, -1.0)):
                pool.memset(col[:, :], value).then_inc(cols_ready, 1)
            pool.wait_ge(cols_ready, 6)

            def over_tiles(run):
                def layer_norm_scale(i, k):
                    slot = slice(k % 2, k % 2 + 1)
                    if k >= 2:
                        pool.wait_ge(run.h_hi_ready, tiles_done(i, k - 2))
                    pool.wait_ge(run.mv_ready, tiles_done(i, k))
                    pool.tensor_tensor(var_eps[:, slot], mv[:, k % 2, 1:2], eps_col[:, :], ALU.add).then_inc(
                        run.norm_step, 1)
                    pool.tensor_tensor(mean_neg[:, slot], mv[:, k % 2, 0:1], minus_col[:, :], ALU.mult).then_inc(
                        run.norm_step, 1)
                    pool.wait_ge(run.norm_step, tiles_done(i, k, NORM_OPS) - 1)
                    pool.tensor_tensor(root[:, slot], var_eps[:, slot], half_neg[:, :], ALU.pow).then_inc(run.norm_step, 1)
                    pool.wait_ge(run.norm_step, tiles_done(i, k, NORM_OPS))
                    pool.tensor_tensor(rstd[:, slot], root[:, slot], h_scale_col[:, :], ALU.mult).then_inc(
                        run.rstd_ready, 1)
                    pool.wait_ge(run.rstd_ready, tiles_done(i, k))
                    pool.tensor_tensor(shift[:, slot], mean_neg[:, slot], rstd[:, slot], ALU.mult).then_inc(
                        run.shift_ready, 1)

                def row_limits(i, k):
                    slot = slice(k % 2, k % 2 + 1)
                    c = cnt[:, k % 4:k % 4 + 1]
                    if k >= 2:
                        pool.wait_ge(run.score_ready, tiles_done(i, k - 2))
                    pool.wait_ge(run.cnt_ready, tiles_done(i, k))
                    pool.tensor_tensor(rest[:, k % 4:k % 4 + 1], n_col[:, :], c, ALU.subtract).then_inc(run.limit_step, 1)
                    pool.tensor_scalar(floor0[:, slot], c, float(N), NO_FLOOR, ALU.is_ge, ALU.mult).then_inc(
                        run.limit_step, 1)
                    pool.tensor_scalar(cap[:, slot], c, CAP_SLOPE, NEG_INF, ALU.mult, ALU.add).then_inc(run.limit_step, 1)
                    pool.wait_ge(run.limit_step, LIMIT_OPS * UNROLL * i + LIMIT_OPS * k + 2)
                    pool.tensor_tensor(floor[:, slot], floor0[:, slot], neg_row[:, 0:1], ALU.add).then_inc(
                        run.limit_step, 1)

                def exponents(i, k):
                    slot = k % 2
                    if k >= 2:
                        pool.wait_ge(run.probs_ready, tiles_done(i, k - 2))
                    pool.wait_ge(run.score_ready, tiles_done(i, k))
                    pool.tensor_tensor(diff[:, slot, 0, :], e_cap[:, slot, :], e_max[:, slot, :],
                                       ALU.subtract).then_inc(run.score_step, 1)
                    pool.tensor_tensor(diff[:, slot, 1, :], neg_row[:, :], e_max[:, slot, :],
                                       ALU.subtract).then_inc(run.score_step, 1)

                def denominators(i, k):
                    slot = k % 2
                    c = cnt[:, k % 4:k % 4 + 1]

                    if k >= 2:
                        pool.wait_ge(run.rden_ready, tiles_done(i, k - 2))
                    pool.wait_ge(run.probs_ready, tiles_done(i, k))
                    pool.tensor_tensor(den_in[:, :], probs[:, slot, 0, :], c.to_broadcast([P, H]), ALU.mult).then_inc(
                        run.denom_step, 1)
                    pool.tensor_tensor(den_out[:, :], probs[:, slot, 1, :],
                                       rest[:, k % 4:k % 4 + 1].to_broadcast([P, H]), ALU.mult).then_inc(run.denom_step, 1)
                    pool.wait_ge(run.denom_step, DENOM_OPS * UNROLL * i + DENOM_OPS * k + 2)
                    pool.tensor_tensor(den[:, slot, :], den_in[:, :], den_out[:, :], ALU.add).then_inc(run.denom_step, 1)

                def step(i, k):
                    if live(k + 2):
                        layer_norm_scale(i, k + 2)
                    if k == -1 and not run.exact:
                        pool.wait_ge(w_max_ready, 1)
                        pool.partition_all_reduce(w_maxall[:, :], w_max1[:, :], P,
                                                  bass.bass_isa.ReduceOp.max).then_inc(w_maxall_ready, 1)
                    if k == TILES + 2 and not run.exact:
                        pool.wait_ge(run.worst_ready, TILES)
                        pool.partition_all_reduce(worst_all[:, :], worst[:, :], P,
                                                  bass.bass_isa.ReduceOp.max).then_inc(worst_all_ready, 1)
                    if live(k - 4):
                        denominators(i, k - 4)
                    if live(k - 3):
                        exponents(i, k - 3)
                    if live(k - 2):
                        row_limits(i, k - 2)

                run_steps(pool, step)

            over_tiles(runs[0])
            exact_run_if_needed(pool, over_tiles)

        @block.scalar
        def _(act):
            def over_tiles(run):
                def split_w_hi():
                    act.wait_ge(w_scale_ready, 1)
                    for c in range(KC):
                        act.activation(w_hi[:, c, :], w_stage[:, c, :], ACT.Copy,
                                       scale=w_scale[:, :]).then_inc(w_hi_ready, 1)

                def elu_exp(i, k):
                    act.wait_ge(run.z_ready, tiles_done(i, k))
                    if k >= 2:
                        act.wait_ge(run.out_ready, tiles_done(i, k - 2))
                    act.activation(g[:, k % 2, :], z[:, k % 2, :, :], ACT.Relu, scale=-1.0).then_inc(
                        run.g_neg_ready, 1)
                    act.wait_ge(run.g_neg_ready, tiles_done(i, k))
                    act.activation(g[:, k % 2, :], g[:, k % 2, :], ACT.Exp, scale=-1.0).then_inc(run.g_exp_ready, 1)

                def normalise(i, k):
                    act.wait_ge(run.shift_ready, tiles_done(i, k))
                    if k >= 2:
                        act.wait_ge(run.h_lo_ready, tiles_done(i, k - 2))
                        act.wait_ge(run.h_turned[k % 2], 16 * rank(i, k, 2))
                    for target, ready in ((h[:, k % 2, 0, :], run.h_hi_ready), (y[:, k % 2, :], run.y_ready)):
                        act.activation(target, x_ring[:, k % 8, :], ACT.Relu, scale=rstd[:, k % 2:k % 2 + 1],
                                       bias=shift[:, k % 2:k % 2 + 1]).then_inc(ready, 1)

                def convert_adj(i, k):
                    act.wait_ge(run.adj_loaded[k % 4], 16 * rank(i, k, 4) + 16)
                    if k >= 2:
                        act.wait_ge(run.adj_turned[k % 2], 16 * rank(i, k, 2))
                        act.wait_ge(run.cnt_ready, tiles_done(i, k - 2))
                    if not run.exact:
                        if k >= 4:
                            act.wait_ge(run.worst_ready, tiles_done(i, k - 4))
                        if k >= 1:
                            act.wait_ge(run.squares_ready, tiles_done(i, k - 1))
                        act.activation(square[:, :], adj_ring[:, k % 4, :], ACT.Square,
                                       accum_out=squares[:, k % 4:k % 4 + 1]).then_inc(run.squares_ready, 1)
                    act.activation(adj_b[:, k % 2, 0, :], adj_ring[:, k % 4, :], ACT.Copy).then_inc(run.adj_ready, 1)

                def softmax_exp(i, k):
                    act.wait_ge(run.score_step, tiles_done(i, k, SCORE_OPS))
                    if k >= 2:
                        act.wait_ge(run.factor_ready, tiles_done(i, k - 2))
                    act.activation(probs[:, k % 2, :, :], diff[:, k % 2, :, :], ACT.Exp).then_inc(run.probs_ready, 1)

                def wh_hi(i, k):
                    act.wait_ge(run.acc_ready, tiles_done(i, k))
                    wh_slot_free(act, run, i, k)
                    for half in range(HALVES):
                        act.activation(wh[:, k // JC % 2, 0, k % JC, half * BANK:(half + 1) * BANK],
                                       acc[:, k % 2, half, :], ACT.Copy,
                                       scale=1.0 / H_SCALE).then_inc(run.wh_hi_ready, 1)

                def step(i, k):
                    if live(k - 2):
                        convert_adj(i, k - 2)
                    if live(k - 5):
                        elu_exp(i, k - 5)
                    if live(k + 2):
                        normalise(i, k + 2)
                    if k == -1 and not run.exact:
                        split_w_hi()
                    if live(k - 3):
                        softmax_exp(i, k - 3)
                    if live(k):
                        wh_hi(i, k)

                run_steps(act, step)

            over_tiles(runs[0])
            exact_run_if_needed(act, over_tiles)

        @block.vector
        def _(dve):
            def over_tiles(run):
                def w_maxima(chunks):
                    for c in chunks:
                        dve.wait_ge(w_loaded[c], 16)
                        dve.tensor_reduce(out=w_max[:, c:c + 1], in_=w_stage[:, c, :], axis=AX.X, op=ALU.max,
                                          apply_absolute_value=True).then_inc(w_stat, 1)

                def w_scale_steps():
                    w_maxima(range(W_EARLY[-1], KC))
                    dve.wait_ge(w_stat, KC)
                    dve.tensor_reduce(out=w_max1[:, :], in_=w_max[:, :], axis=AX.X, op=ALU.max).then_inc(
                        w_max_ready, 1)
                    dve.wait_ge(w_maxall_ready, 1)
                    dve.tensor_scalar(w_pow[:, :].bitcast(I32), w_maxall[:, :].bitcast(I32), 0x7F800000, None,
                                      ALU.bitwise_and).then_inc(w_stat, 1)
                    dve.wait_ge(w_stat, KC + 1)
                    dve.tensor_scalar(w_powc[:, :], w_pow[:, :], 2.0 ** -110, 2.0 ** 126, ALU.max,
                                      ALU.min).then_inc(w_stat, 1)
                    dve.wait_ge(w_stat, KC + 2)
                    dve.reciprocal(w_rec[:, :], w_powc[:, :]).then_inc(w_stat, 1)
                    dve.wait_ge(w_stat, KC + 3)
                    dve.tensor_scalar(w_scale[:, :], w_rec[:, :], 16.0, None, ALU.mult).then_inc(w_scale_ready, 1)
                    dve.tensor_scalar(w_inv[:, :], w_powc[:, :], 1.0 / 16.0, None, ALU.mult).then_inc(w_stat, 1)

                def split_w_lo():
                    dve.wait_ge(w_scale_ready, 1)
                    for c in range(KC):
                        dve.wait_ge(w_hi_ready, c + 1)
                        dve.scalar_tensor_tensor(out=w_lo[:, c, :], in0=w_stage[:, c, :], scalar=w_scale[:, :],
                                                 in1=w_hi[:, c, :], op0=ALU.mult, op1=ALU.subtract).then_inc(
                            w_lo_ready, 1)
                    dve.wait_ge(a_loaded, 16)
                    a_heads = a_sb[:, :].rearrange("p (h f) -> p h f", h=H)
                    dve.tensor_tensor(a_sum[:, :, :], a_heads[:, :, 0:F], a_heads[:, :, F:F2], ALU.add).then_inc(
                        a_added, 1)
                    dve.wait_ge(w_stat, KC + 4)
                    dve.wait_ge(a_added, 1)
                    dve.tensor_scalar(a_sum[:, :, :], a_sum[:, :, :], w_inv[:, :], 1.0 / H_SCALE, ALU.mult,
                                      ALU.mult).then_inc(a_ready, 1)

                def wh_lo(i, k):
                    wh_slot_free(dve, run, i, k)
                    for half in range(HALVES):
                        cols = slice(half * BANK, (half + 1) * BANK)
                        dve.wait_ge(run.wh_hi_ready, tiles_done(i, k, 2) - 1 + half)
                        dve.scalar_tensor_tensor(out=wh[:, k // JC % 2, 1, k % JC, cols], in0=acc[:, k % 2, half, :],
                                                 scalar=1.0 / H_SCALE, in1=wh[:, k // JC % 2, 0, k % JC, cols],
                                                 op0=ALU.mult, op1=ALU.subtract).then_inc(run.wh_lo_ready, 1)

                def score_products(i, k):
                    if k == 0:
                        dve.wait_ge(a_ready, 1)
                    acc_heads = acc[:, k % 2, :, :].rearrange("p a (h f) -> p (a h) f", f=F)
                    dve.tensor_tensor(prod[:, :, :], acc_heads, a_sum[:, :, :], ALU.mult).then_inc(run.prod_ready, 1)

                def score_sums(i, k):
                    dve.wait_ge(run.prod_ready, tiles_done(i, k))
                    dve.tensor_reduce(out=e_raw[:, :], in_=prod[:, :, :], axis=AX.X, op=ALU.add).then_inc(
                        run.e_raw_ready, 1)

                def leaky_relu(i, k):
                    dve.wait_ge(run.e_raw_ready, tiles_done(i, k))
                    dve.scalar_tensor_tensor(out=e_lr[:, k % 4, :], in0=e_raw[:, :], scalar=ALPHA, in1=e_raw[:, :],
                                             op0=ALU.mult, op1=ALU.max).then_inc(run.e_ready, 1)

                def scale_rows(i, k):
                    dve.wait_ge(run.agg_ready, tiles_done(i, k))
                    dve.wait_ge(run.factor_ready, tiles_done(i, k))
                    if k >= 2:
                        dve.wait_ge(run.g_neg_ready, tiles_done(i, k - 2))
                    agg_heads = agg[:, k % 2, :, :].rearrange("p a (h f) -> p (a h) f", f=F)
                    row_factor = factor[:, k % 2, :].unsqueeze(2).to_broadcast([P, H, F])
                    dve.tensor_tensor(z[:, k % 2, :, :], agg_heads, row_factor, ALU.mult).then_inc(run.z_ready, 1)

                def add_positive(i, k):
                    dve.wait_ge(run.z_ready, tiles_done(i, k))
                    z_row = z[:, k % 2, :, :].rearrange("p h f -> p (h f)")
                    dve.scalar_tensor_tensor(out=r[:, k % 2, :], in0=z_row, scalar=0.0, in1=x_ring[:, k % 8, :],
                                             op0=ALU.max, op1=ALU.add).then_inc(run.x_used, 1)

                def add_negative(i, k):
                    dve.wait_ge(run.g_exp_ready, tiles_done(i, k))
                    dve.wait_ge(run.x_used, tiles_done(i, k))
                    if k >= 2:
                        dve.wait_ge(run.stored[k % 2], 16 * rank(i, k, 2))
                    dve.scalar_tensor_tensor(out=out_sb[:, k % 2, :], in0=g[:, k % 2, :], scalar=-1.0,
                                             in1=r[:, k % 2, :], op0=ALU.add, op1=ALU.add).then_inc(run.out_ready, 1)

                def row_stats(i, k):
                    dve.wait_ge(run.x_loaded[k % 8], 16 * rank(i, k, 8) + 16)
                    for half in range(HALVES):
                        dve.bn_stats(stats[:, k % 2, half, :],
                                     x_ring[:, k % 8, half * BANK:(half + 1) * BANK]).then_inc(run.stats_ready, 1)

                def row_moments(i, k):
                    dve.bn_aggr(mv[:, k % 2, :], stats[:, k % 2, :, :].rearrange("p a b -> p (a b)")).then_inc(
                        run.mv_ready, 1)

                def split_lo(i, k):
                    dve.wait_ge(run.y_ready, tiles_done(i, k))
                    dve.wait_ge(run.h_hi_ready, tiles_done(i, k))
                    if k >= 2:
                        dve.wait_ge(run.h_turned[k % 2], 16 * rank(i, k, 2))
                    dve.tensor_tensor(h[:, k % 2, 1, :], y[:, k % 2, :], h[:, k % 2, 0, :], ALU.subtract).then_inc(
                        run.h_lo_ready, 1)

                def count_neighbours(i, k):
                    dve.wait_ge(run.adj_ready, tiles_done(i, k))
                    if k >= 4:
                        dve.wait_ge(run.denom_step, tiles_done(i, k - 4, DENOM_OPS))
                    dve.tensor_scalar(adj_mask[:, :], adj_b[:, k % 2, 0, :], 0.0, 0.0, ALU.not_equal, ALU.add,
                                      accum_out=cnt[:, k % 4:k % 4 + 1]).then_inc(run.cnt_ready, 1)

                def limited_scores(i, k):
                    dve.wait_ge(run.limit_step, tiles_done(i, k, LIMIT_OPS))
                    dve.wait_ge(run.e_ready, tiles_done(i, k))
                    if k >= 2:
                        dve.wait_ge(run.score_step, tiles_done(i, k - 2, SCORE_OPS))
                    slot = slice(k % 2, k % 2 + 1)
                    dve.tensor_scalar(e_cap[:, k % 2, :], e_lr[:, k % 4, :], cap[:, slot], None, ALU.min)
                    dve.tensor_scalar(e_max[:, k % 2, :], e_lr[:, k % 4, :], cap[:, slot], floor[:, slot], ALU.min,
                                      ALU.max).then_inc(run.score_ready, 1)

                def check_adj(i, k):
                    dve.wait_ge(run.squares_ready, tiles_done(i, k))
                    if k >= 1:
                        dve.wait_ge(run.worst_ready, tiles_done(i, k - 1))
                    else:
                        dve.wait_ge(worst_zeroed, 1)
                    dve.tensor_tensor(worst[:, :], worst[:, :], squares[:, k % 4:k % 4 + 1], ALU.max).then_inc(
                        run.worst_ready, 1)

                def adj_remainders(i, k):
                    dve.wait_ge(run.adj_ready, tiles_done(i, k))
                    if k >= 2:
                        dve.wait_ge(run.adj_turned[k % 2], 16 * rank(i, k, 2))
                    dve.tensor_tensor(adj_rest[:, :], adj_ring[:, k % 4, :], adj_b[:, k % 2, 0, :],
                                      ALU.subtract).then_inc(run.resid_ready, 1)
                    dve.wait_ge(run.resid_ready, tiles_done(i, k))
                    dve.tensor_copy(adj_b[:, k % 2, 1, :], adj_rest[:, :]).then_inc(run.mid_ready, 1)
                    dve.wait_ge(run.mid_ready, tiles_done(i, k))
                    dve.tensor_tensor(adj_b[:, k % 2, 2, :], adj_rest[:, :], adj_b[:, k % 2, 1, :],
                                      ALU.subtract).then_inc(run.low_ready, 1)

                def invert_denominator(i, k):
                    dve.wait_ge(run.denom_step, tiles_done(i, k, DENOM_OPS))
                    dve.reciprocal(rden[:, :], den[:, k % 2, :]).then_inc(run.rden_ready, 1)

                def row_factors(i, k):
                    dve.wait_ge(run.rden_ready, tiles_done(i, k))
                    if k >= 1:
                        dve.wait_ge(run.z_ready, tiles_done(i, k - 1))
                    dve.scalar_tensor_tensor(out=factor[:, k % 2, :], in0=rden[:, :], scalar=w_inv[:, :],
                                             in1=probs[:, k % 2, 0, :], op0=ALU.mult, op1=ALU.mult).then_inc(
                        run.factor_ready, 1)

                def step(i, k):
                    if live(k + 2):
                        row_stats(i, k + 2)
                        dve.wait_ge(run.stats_ready, tiles_done(i, k + 2, 2))
                    if live(k - 1):
                        wh_lo(i, k - 1)
                    if live(k + 2):
                        row_moments(i, k + 2)
                    if live(k - 1):
                        score_products(i, k - 1)
                    if live(k - 5):
                        scale_rows(i, k - 5)
                    if k < 0 and not run.exact:
                        w_maxima(range(W_EARLY[k + 2], W_EARLY[k + 3]))
                    if live(k - 1):
                        score_sums(i, k - 1)
                    if live(k - 5):
                        add_positive(i, k - 5)
                    if live(k - 3):
                        limited_scores(i, k - 3)
                    if live(k - 2):
                        count_neighbours(i, k - 2)
                        if run.exact:
                            adj_remainders(i, k - 2)
                        else:
                            check_adj(i, k - 2)
                    if live(k - 4):
                        invert_denominator(i, k - 4)
                    if live(k - 6):
                        add_negative(i, k - 6)
                    if live(k - 1):
                        leaky_relu(i, k - 1)
                    if live(k - 4):
                        row_factors(i, k - 4)
                    if k == TILES + 3 and not run.exact:
                        dve.wait_ge(worst_all_ready, 1)
                        dve.tensor_scalar(adj_flag[:, :], worst_all[:, :], EXACT_SQUARES, None,
                                          ALU.is_gt).then_inc(flag_ready, 1)
                    if k == -1 and not run.exact:
                        w_scale_steps()
                    if live(k + 2):
                        split_lo(i, k + 2)
                    if k == -1 and not run.exact:
                        split_w_lo()

                run_steps(dve, step)

            dve.memset(worst[:, :], 0.0).then_inc(worst_zeroed, 1)
            over_tiles(runs[0])
            exact_run_if_needed(dve, over_tiles)

        @block.tensor
        def _(pe):
            def over_tiles(run):
                def project(i, k):
                    pe.wait_ge(run.h_turned[k % 2], 16 * rank(i, k, 2) + 16)
                    if k >= 2:
                        pe.wait_ge(run.prod_ready, tiles_done(i, k - 2))
                    for c in range(KC):
                        if k == 0:
                            pe.wait_ge(w_hi_ready, c + 1)
                            pe.wait_ge(w_lo_ready, c + 1)
                        for h_part, w_part in ((0, w_hi), (0, w_lo), (1, w_hi)):
                            for half in range(HALVES):
                                last = pe.matmul(acc[:, k % 2, half, :], hT[:, k % 2, h_part, c, :],
                                                 w_part[:, c, half * BANK:(half + 1) * BANK],
                                                 start=(c == 0 and h_part == 0 and w_part is w_hi),
                                                 stop=(c == KC - 1 and h_part == 1))
                    last.then_inc(run.acc_ready, 1)

                def aggregate(i, k):
                    pe.wait_ge(run.adj_turned[k % 2], 16 * rank(i, k, 2) + 16)
                    if k % JC == 0:
                        pe.wait_ge(run.wh_lo_ready, 2 * UNROLL * i + 2 * JC * (k // JC + 1))
                    if k >= 2:
                        pe.wait_ge(run.z_ready, tiles_done(i, k - 2))
                    for c in range(JC):
                        for adj_part in range(run.parts):
                            for part in range(2):
                                for half in range(HALVES):
                                    last = pe.matmul(agg[:, k % 2, half, :], adjT[:, k % 2, adj_part, c, :],
                                                     wh[:, k // JC % 2, part, c, half * BANK:(half + 1) * BANK],
                                                     start=(c == 0 and adj_part == 0 and part == 0),
                                                     stop=(c == JC - 1 and adj_part == run.parts - 1 and part == 1))
                    last.then_inc(run.agg_ready, 1)

                def step(i, k):
                    if live(k):
                        project(i, k)
                    if live(k - 4):
                        aggregate(i, k - 4)

                run_steps(pe, step)

            over_tiles(runs[0])
            exact_run_if_needed(pe, over_tiles)


_INS = ["x", "adj", "L0_gnn_W", "L0_gnn_a"]


def kernel(**inputs):
    import numpy as _np
    import concourse.bacc as _bacc
    from concourse import mybir as _mybir
    from concourse.bass_utils import run_bass_kernel_spmd as _run

    nc = _bacc.Bacc("TRN2", target_bir_lowering=False, num_devices=1)
    arrays, args = {}, []
    for name in _INS:
        arr = _np.ascontiguousarray(inputs[name])
        arrays[f"in_{name}"] = arr
        args.append(nc.dram_tensor(f"in_{name}", arr.shape, _mybir.dt.from_np(arr.dtype),
                                   kind="ExternalInput").ap())
    shape = _np.shape(inputs["x"])
    args.append(nc.dram_tensor("out", shape, _mybir.dt.float32, kind="ExternalOutput").ap())
    gat_layer_kernel(nc, *args)
    result = _run(nc, [arrays], core_ids=[0])
    return result.results[0]["out"]
```
